# Optimizing a Trainium2 kernel written in Bass

```python
import numpy as np
import jax
import jax.numpy as jnp

def _softmax(x, axis=-1):
    return jax.nn.softmax(x, axis=axis)

def _gelu(x):
    return jax.nn.gelu(x, approximate=True)

def _silu(x):
    return jax.nn.silu(x)

def _sigmoid(x):
    return jax.nn.sigmoid(x)

def _layernorm(x, axis=-1, eps=1e-05):
    m = jnp.mean(x, axis=axis, keepdims=True)
    v = jnp.var(x, axis=axis, keepdims=True)
    return (x - m) / jnp.sqrt(v + eps)

def _scatter_add(tgt, idx, src, axis=0):
    return tgt.at[idx].add(src)

def _segment_sum(src, seg, n):
    return jax.ops.segment_sum(src, seg, n)
kernel_name = 'mk_adj_preln_d1_adj_r2_3eb7bd'

def setup_inputs(seed: int=0):
    np.random.seed(seed)
    _w = jnp.asarray

    def _rec_inputs():
        import jax
        import jax.numpy as jnp
        _gk = jax.random.key(seed)
        x = -0.0002928 + 1 * jax.random.normal(jax.random.fold_in(_gk, 1), (4096, 256), jnp.float32)
        _w = (1.0 + jnp.arange(4096, dtype=jnp.float32)) ** (-0.5)
        _w = _w / _w.mean()
        _pij = jnp.clip(0.000976562 * _w[:, None] * _w[None, :], 0.0, 1.0)
        _a = jax.random.uniform(jax.random.fold_in(_gk, 2), (4096, 4096)) < _pij
        adj = _a.astype(jnp.int32)
        return (x, adj)
    x, adj = _rec_inputs()

    def _L0_gnn_setup():
        import jax, jax.numpy as jnp
        import numpy as np
        N, D_IN, D_OUT = (4096, 256, 256)
        key = jax.random.key(seed)
        ks = jax.random.split(key, 8)
        scale_in = 1.0 / np.sqrt(D_IN)
        scale_cat = 1.0 / np.sqrt(2 * D_OUT)
        return {'x': jax.random.normal(ks[0], (N, D_IN), dtype=jnp.float32), 'adj': jax.random.randint(ks[1], (N, N), 0, 2, dtype=jnp.int32), 'W_self': jax.random.uniform(ks[2], (D_IN, D_OUT), jnp.float32, -scale_in, scale_in), 'b_self': jax.random.uniform(ks[3], (D_OUT,), jnp.float32, -scale_in, scale_in), 'W_nb': jax.random.uniform(ks[4], (D_IN, D_OUT), jnp.float32, -scale_in, scale_in), 'b_nb': jax.random.uniform(ks[5], (D_OUT,), jnp.float32, -scale_in, scale_in), 'W_comb': jax.random.uniform(ks[6], (2 * D_OUT, D_OUT), jnp.float32, -scale_cat, scale_cat), 'b_comb': jax.random.uniform(ks[7], (D_OUT,), jnp.float32, -scale_cat, scale_cat)}
    _L0_gnn_all = _L0_gnn_setup()
    _L0_gnn_in = {k: v for k, v in _L0_gnn_all.items() if k in ('W_self', 'b_self', 'W_nb', 'b_nb', 'W_comb', 'b_comb')}
    del _L0_gnn_all
    return {'x': x, 'adj': adj, 'L0_gnn_W_self': _L0_gnn_in['W_self'], 'L0_gnn_b_self': _L0_gnn_in['b_self'], 'L0_gnn_W_nb': _L0_gnn_in['W_nb'], 'L0_gnn_b_nb': _L0_gnn_in['b_nb'], 'L0_gnn_W_comb': _L0_gnn_in['W_comb'], 'L0_gnn_b_comb': _L0_gnn_in['b_comb']}

def reference(x, adj, L0_gnn_W_self, L0_gnn_b_self, L0_gnn_W_nb, L0_gnn_b_nb, L0_gnn_W_comb, L0_gnn_b_comb):
    import jax
    import jax.numpy as jnp

    def _L0_gnn_ref(x, adj, W_self, b_self, W_nb, b_nb, W_comb, b_comb):
        import jax, jax.numpy as jnp
        import numpy as np
        N, D_IN, D_OUT = (4096, 256, 256)
        mask = (adj > 0).astype(x.dtype)
        deg = jnp.sum(mask, axis=1, keepdims=True)
        agg = mask @ x / jnp.maximum(deg, 1.0)
        self_f = x @ W_self + b_self
        nb_f = agg @ W_nb + b_nb
        combined = jnp.concatenate([self_f, nb_f], axis=-1)
        out = combined @ W_comb + b_comb
        return jax.nn.relu(out)
    h = jnp.maximum(_layernorm(x, axis=-1), 0.0)
    x = x + _L0_gnn_ref(h, adj, L0_gnn_W_self, L0_gnn_b_self, L0_gnn_W_nb, L0_gnn_b_nb, L0_gnn_W_comb, L0_gnn_b_comb)
    return x

_drawn_inputs = setup_inputs


def setup_inputs(seed=0):
    import zlib

    import numpy as np

    out = dict(_drawn_inputs(seed))
    spreads = {}
    factors = {'L0_gnn_b_self': 5.977, 'L0_gnn_b_nb': 5.284, 'L0_gnn_b_comb': 3.14}
    for name, (base, spread) in spreads.items():
        noise = np.random.default_rng([zlib.crc32(name.encode()), seed]).standard_normal(out[name].shape)
        drawn = base * np.exp(spread * noise) if base else spread * noise
        out[name] = jnp.asarray(drawn.astype(out[name].dtype))
    for name, factor in factors.items():
        out[name] = (out[name] * factor).astype(out[name].dtype)
    return out
```

```python
from contextlib import ExitStack

import concourse.bass as bass
from concourse import mybir

ALU = mybir.AluOpType
ACT = mybir.ActivationFunctionType
F32 = mybir.dt.float32
F16 = mybir.dt.float16
I32 = mybir.dt.int32

P = 128
EPS = 1e-5
LIMIT = 2048.0
TINY = 1e-30

GROUP = 4
BODY = 8
MASKS = 4
RAWS = 2 * MASKS
WEIGHT_LOADS = 5


def gnn_kernel(nc, x, adj_t, w_self_t, w_nb_t, w_comb, b_hidden, b_comb, out):
    N, D = x.shape
    T = N // P
    KC = D // P
    HALF = T * P // 2
    DW = D + 1

    x_dram = x.rearrange("(p t) d -> p t d", p=P)
    out_dram = out.rearrange("(p t) d -> p t d", p=P)

    with ExitStack() as ctx:
        def sb(name, shape, dt):
            return ctx.enter_context(nc.sbuf_tensor(name, shape, dt))

        def psum(name, shape, dt):
            return ctx.enter_context(nc.psum_tensor(name, shape, dt))

        def sem(name):
            return ctx.enter_context(nc.semaphore(name))

        x_sb = sb("x_sb", [P, T, D], F32)
        s_sb = sb("s_sb", [P, T, D], F32)
        z_hi = sb("z_hi", [P, T, DW], F16)
        z_lo = sb("z_lo", [P, T, D], F16)
        raw = sb("raw", [P, RAWS, HALF], I32)
        mask = sb("mask", [P, MASKS, 2 * HALF], F16)
        mask_halves = mask[:, :, :].rearrange("p s (e n) -> p (s e) n", e=2)
        w_fold = sb("w_fold", [P, KC, 2 * D], F32)
        unscale = sb("unscale", [P, D], F32)
        rescale = sb("rescale", [P, D], F32)
        bias = sb("bias", [P, D], F32)
        ident = sb("ident", [P, P], F32)
        ones = sb("ones", [P, P], F32)
        h = sb("h", [P, 2, D], F32)
        h_t = sb("h_t", [P, 2, KC, P], F32)
        moments = sb("moments", [P, GROUP, 6], F32)
        mean_sum = sb("mean_sum", [P, GROUP], F32)
        mean_gap = sb("mean_gap", [P, GROUP], F32)
        square_sum = sb("square_sum", [P, GROUP], F32)
        within = sb("within", [P, GROUP], F32)
        between = sb("between", [P, GROUP], F32)
        var_eps = sb("var_eps", [P, GROUP], F32)
        std = sb("std", [P, GROUP], F32)
        r0 = sb("r0", [P, GROUP], F32)
        newton_a = sb("newton_a", [P, GROUP], F32)
        newton_b = sb("newton_b", [P, GROUP], F32)
        rstd = sb("rstd", [P, 2, GROUP], F32)
        shift = sb("shift", [P, 2, GROUP], F32)
        deg = sb("deg", [P, 1], F32)
        rdeg = sb("rdeg", [P, 1], F32)
        mean_nb = sb("mean_nb", [P, D], F32)
        pre = sb("pre", [P, D], F32)
        b_cols = sb("b_cols", [P, 2 * KC], F32)

        w_stage = mask[:, MASKS - 1, :].bitcast(F32)
        ws_t = w_stage[:, 0:KC * D].rearrange("p (c n) -> p c n", c=KC)
        wn_t = w_stage[:, KC * D:2 * KC * D].rearrange("p (c n) -> p c n", c=KC)
        wc = w_stage[:, 2 * KC * D:4 * KC * D].rearrange("p (c n) -> p c n", c=2 * KC)
        stage2 = mask[:, MASKS - 2, :].bitcast(F32)
        abs_wn = stage2[:, 0:KC * D].rearrange("p (c n) -> p c n", c=KC)
        b_wide = stage2[:, KC * D:KC * D + 2 * KC * P].rearrange("p (c n) -> p c n", c=2 * KC)
        b_comb_bc = stage2[:, 2 * KC * D:2 * KC * D + D]

        acc = [psum(f"acc{i}", [P, 512], F32) for i in range(2)]
        ps_ht = [psum(f"ps_ht{i}", [P, 512], F32) for i in range(2)]
        ps_zs = [psum(f"ps_zs{i}", [P, 512], F32) for i in range(2)]
        ps_fold = ps_zs
        ps_colsum, ps_bias = acc

        x_landed = [sem(f"x_landed{i}") for i in range(2)]
        weights_landed = sem("weights_landed")
        early_landed = [sem(f"early_landed{i}") for i in range(2)]
        raw_landed = [sem(f"raw_landed{i}") for i in range(RAWS)]
        ident_zero = sem("ident_zero")
        ident_ready = sem("ident_ready")
        degree_ones_ready = sem("degree_ones_ready")
        ones_ready = sem("ones_ready")
        b_wide_ready = sem("b_wide_ready")
        folded = sem("folded")
        abs_ready = sem("abs_ready")
        colsum_ready = sem("colsum_ready")
        unscale_ready = sem("unscale_ready")
        rescale_ready = sem("rescale_ready")
        bias_summed = sem("bias_summed")
        bias_ready = sem("bias_ready")
        w_ready = sem("w_ready")
        moments_ready = sem("moments_ready")
        sums_ready = sem("sums_ready")
        parts_ready = sem("parts_ready")
        var_ready = sem("var_ready")
        std_ready = sem("std_ready")
        r0_ready = sem("r0_ready")
        newton_a_ready = sem("newton_a_ready")
        newton_b_ready = sem("newton_b_ready")
        rstd_ready = sem("rstd_ready")
        shift_ready = sem("shift_ready")
        h_ready = sem("h_ready")
        ht_in_psum = sem("ht_in_psum")
        ht_ready = sem("ht_ready")
        zs_in_psum = sem("zs_in_psum")
        hi_ready = sem("hi_ready")
        zs_taken = sem("zs_taken")
        converted = sem("converted")
        tile_summed = sem("tile_summed")
        deg_ready = sem("deg_ready")
        rdeg_ready = sem("rdeg_ready")
        acc_taken = sem("acc_taken")
        pre_ready = sem("pre_ready")
        out_ready = sem("out_ready")
        stored = sem("stored")

        def row(tensor, t):
            if isinstance(t, int):
                return tensor[:, t, :]
            return tensor[:, bass.ds(t, 1), :].rearrange("p a n -> p (a n)")

        block = ctx.enter_context(nc.Block())

        @block.sync
        def _(sp):
            def load_x(group):
                tiles = slice(group * GROUP, (group + 1) * GROUP)
                sp.dma_start(x_sb[:, tiles, :], x_dram[:, tiles, :]).then_inc(x_landed[group % 2], 16)

            load_x(0)
            sp.dma_start(ws_t, w_self_t.rearrange("(c p) n -> p c n", p=P)).then_inc(weights_landed, 16)
            sp.dma_start(wn_t, w_nb_t.rearrange("(c p) n -> p c n", p=P)).then_inc(weights_landed, 16)
            sp.dma_start(wc, w_comb.rearrange("(c p) n -> p c n", p=P)).then_inc(weights_landed, 16)
            sp.dma_start(b_cols[:, :], b_hidden).then_inc(weights_landed, 16)
            sp.dma_start(b_comb_bc, b_comb.broadcast_to([P, D])).then_inc(weights_landed, 16)
            load_x(1)
            for group in range(2, T // GROUP):
                sp.wait_ge(x_landed[group % 2], 16 * (group // 2))
                load_x(group)
            for half in range(RAWS):
                if half >= 2:
                    sp.wait_ge(early_landed[half % 2], 16 * (half // 2))
                sp.dma_start(raw[:, half, :], adj_t[half]).then_inc(early_landed[half % 2], 16)
            with sp.Fori(1, T // MASKS) as turn:
                for slot in range(RAWS):
                    sp.wait_ge(converted, turn * RAWS + (slot + 1 - RAWS))
                    sp.dma_start(raw[:, slot, :],
                                 adj_t[bass.ds(turn * RAWS + slot, 1)].rearrange("a p n -> p (a n)")
                                 ).then_inc(raw_landed[slot], 16)

        @block.gpsimd
        def _(pool):
            nc.gpsimd.memset(ident[:], 0.0).then_inc(ident_zero, 1)
            pool.wait_ge(ident_zero, 1)
            nc.gpsimd.affine_select(out=ident[:], in_=ident[:], compare_op=ALU.not_equal, fill=1.0, base=0,
                                    pattern=[[-1, P]], channel_multiplier=1).then_inc(ident_ready, 1)
            nc.gpsimd.memset(z_hi[:, :, D:DW], 1.0).then_inc(degree_ones_ready, 1)

        @block.scalar
        def _(act):
            def normalise(t, k):
                pair, q = k // GROUP, k % GROUP
                nc.scalar.activation(h[:, k % 2, :], row(x_sb, t), ACT.Relu, bias=shift[:, pair, q:q + 1],
                                     scale=rstd[:, pair, q:q + 1]).then_inc(h_ready, 1)

            def take_ht(t, b):
                act.wait_ge(ht_in_psum, t + 1)
                nc.scalar.copy(h_t[:, b].rearrange("p c n -> p (c n)"), ps_ht[b][:, 0:D]).then_inc(ht_ready, 1)

            def take_hi(t, b):
                act.wait_ge(zs_in_psum, t + 1)
                nc.scalar.copy(row(z_hi, t)[:, 0:D], ps_zs[b][:, 0:D]).then_inc(hi_ready, 1)

            def project(turn):
                peeled = isinstance(turn, int)
                for k in range(BODY):
                    t = turn * BODY + k
                    if k % GROUP == 0:
                        group = turn * (BODY // GROUP) + k // GROUP
                        act.wait_ge(var_ready, group + 1)
                        nc.scalar.activation(std[:], var_eps[:], ACT.Sqrt).then_inc(std_ready, 1)
                        act.wait_ge(shift_ready, group + 1)
                    if not peeled or k >= 2:
                        act.wait_ge(ht_in_psum, t - 1)
                    normalise(t, k)
                    if not peeled or k >= 3:
                        act.wait_ge(zs_in_psum, t - 2)
                    if not peeled or k >= 1:
                        take_ht(t - 1, (k - 1) % 2)
                    if not peeled or k >= 2:
                        take_hi(t - 2, k % 2)

            act.wait_ge(folded, 1)
            for c in range(KC):
                last = nc.scalar.activation(abs_wn[:, c, :], ps_fold[c][:, 0:D], ACT.Abs)
            last.then_inc(abs_ready, 1)
            project(0)
            with act.Fori(1, T // BODY) as turn:
                project(turn)
            act.wait_ge(zs_in_psum, T - 2)
            take_ht(T - 1, 1)
            take_hi(T - 2, 0)
            take_hi(T - 1, 1)
            with act.Fori(0, T // MASKS - 1) as turn:
                act.wait_ge(out_ready, (turn + 1) * MASKS)
                act.dma_start(out_dram[:, bass.ds(turn * MASKS, MASKS), :],
                              x_sb[:, bass.ds(turn * MASKS, MASKS), :]).then_inc(stored, 16)
            for t in range(T - MASKS, T):
                act.wait_ge(out_ready, t + 1)
                act.dma_start(out_dram[:, t, :], x_sb[:, t, :]).then_inc(stored, 16)
            act.wait_ge(stored, 16 * (T // MASKS - 1 + MASKS))

        @block.vector
        def _(dve):
            def statistics(group, pair, peeled):
                for q in range(GROUP):
                    last = nc.vector.bn_stats(moments[:, q, :], row(x_sb, group * GROUP + q))
                last.then_inc(moments_ready, 1)
                dve.wait_ge(moments_ready, group + 1)
                nc.vector.tensor_tensor(mean_sum[:], moments[:, :, 1], moments[:, :, 4], ALU.add)
                nc.vector.tensor_tensor(mean_gap[:], moments[:, :, 1], moments[:, :, 4], ALU.subtract)
                nc.vector.tensor_tensor(square_sum[:], moments[:, :, 2], moments[:, :, 5],
                                        ALU.add).then_inc(sums_ready, 1)
                dve.wait_ge(sums_ready, group + 1)
                nc.vector.tensor_scalar(within[:], square_sum[:], 1.0 / D, EPS, ALU.mult, ALU.add)
                nc.vector.scalar_tensor_tensor(out=between[:], in0=mean_gap[:], scalar=0.25, in1=mean_gap[:],
                                               op0=ALU.mult, op1=ALU.mult).then_inc(parts_ready, 1)
                dve.wait_ge(parts_ready, group + 1)
                nc.vector.tensor_tensor(var_eps[:], within[:], between[:], ALU.add).then_inc(var_ready, 1)
                dve.wait_ge(std_ready, group + 1)
                nc.vector.reciprocal(r0[:], std[:]).then_inc(r0_ready, 1)
                dve.wait_ge(r0_ready, group + 1)
                nc.vector.tensor_tensor(newton_a[:], var_eps[:], r0[:], ALU.mult).then_inc(newton_a_ready, 1)
                dve.wait_ge(newton_a_ready, group + 1)
                nc.vector.scalar_tensor_tensor(out=newton_b[:], in0=newton_a[:], scalar=-0.5, in1=r0[:],
                                               op0=ALU.mult, op1=ALU.mult).then_inc(newton_b_ready, 1)
                dve.wait_ge(newton_b_ready, group + 1)
                if not peeled:
                    dve.wait_ge(h_ready, (group - 1) * GROUP)
                nc.vector.scalar_tensor_tensor(out=rstd[:, pair, :], in0=newton_b[:], scalar=1.5, in1=r0[:],
                                               op0=ALU.add, op1=ALU.mult).then_inc(rstd_ready, 1)
                dve.wait_ge(rstd_ready, group + 1)
                nc.vector.scalar_tensor_tensor(out=shift[:, pair, :], in0=mean_sum[:], scalar=-0.5,
                                               in1=rstd[:, pair, :], op0=ALU.mult,
                                               op1=ALU.mult).then_inc(shift_ready, 1)

            def take_zs(group):
                for q in range(GROUP):
                    t, b = group * GROUP + q, q % 2
                    dve.wait_ge(hi_ready, t + 1)
                    nc.vector.tensor_tensor(row(s_sb, t), ps_zs[b][:, D:2 * D], bias[:], ALU.add)
                    nc.vector.tensor_tensor(row(z_lo, t), ps_zs[b][:, 0:D], row(z_hi, t)[:, 0:D],
                                            ALU.subtract).then_inc(zs_taken, 1)

            def to_mask(half):
                nc.vector.tensor_scalar(row(mask_halves, half), row(raw, half), 0, None,
                                        ALU.is_gt).then_inc(converted, 1)

            nc.vector.memset(ones[:], 1.0).then_inc(ones_ready, 1)
            dve.wait_ge(x_landed[0], 16)
            statistics(0, 0, True)
            dve.wait_ge(ones_ready, 1)
            dve.wait_ge(weights_landed, 16 * WEIGHT_LOADS)
            for c in range(2 * KC):
                last = nc.vector.tensor_scalar(b_wide[:, c, :], ones[:], b_cols[:, c:c + 1], None, ALU.mult)
            last.then_inc(b_wide_ready, 1)
            dve.wait_ge(bias_summed, 1)
            nc.vector.tensor_tensor(bias[:], ps_bias[:, 0:D], b_comb_bc, ALU.add).then_inc(bias_ready, 1)
            dve.wait_ge(colsum_ready, 1)
            nc.vector.tensor_scalar(unscale[:], ps_colsum[:, 0:D], TINY, 1.0 / LIMIT,
                                    ALU.max, ALU.mult).then_inc(unscale_ready, 1)
            dve.wait_ge(unscale_ready, 1)
            nc.vector.reciprocal(rescale[:], unscale[:]).then_inc(rescale_ready, 1)
            dve.wait_ge(rescale_ready, 1)
            dve.wait_ge(folded, 1)
            for c in range(KC):
                nc.vector.tensor_tensor(w_fold[:, c, 0:D], ps_fold[c][:, 0:D], rescale[:], ALU.mult)
                last = nc.vector.tensor_copy(w_fold[:, c, D:2 * D], ps_fold[c][:, D:2 * D])
            last.then_inc(w_ready, 1)
            dve.wait_ge(bias_ready, 1)
            dve.wait_ge(x_landed[1], 16)
            statistics(1, 1, True)
            take_zs(0)
            dve.wait_ge(early_landed[0], 16)
            to_mask(0)
            with dve.Fori(1, T // BODY) as turn:
                dve.wait_ge(x_landed[0], turn * 16 + 16)
                statistics(turn * 2, 0, False)
                take_zs(turn * 2 - 1)
                dve.wait_ge(early_landed[1], turn * 16)
                to_mask(turn * 2 - 1)
                dve.wait_ge(x_landed[1], turn * 16 + 16)
                statistics(turn * 2 + 1, 1, False)
                take_zs(turn * 2)
                dve.wait_ge(early_landed[0], turn * 16 + 16)
                to_mask(turn * 2)
            take_zs(T // GROUP - 1)
            dve.wait_ge(early_landed[1], 16 * RAWS // 2)
            to_mask(RAWS - 1)

            def finish(t, b):
                dve.wait_ge(tile_summed, t + 1)
                nc.vector.tensor_scalar(deg[:], acc[b][:, D:DW], 1.0, None, ALU.max).then_inc(deg_ready, 1)
                dve.wait_ge(deg_ready, t + 1)
                nc.vector.reciprocal(rdeg[:], deg[:]).then_inc(rdeg_ready, 1)
                dve.wait_ge(rdeg_ready, t + 1)
                nc.vector.scalar_tensor_tensor(out=mean_nb[:], in0=acc[b][:, 0:D], scalar=rdeg[:], in1=unscale[:],
                                               op0=ALU.mult, op1=ALU.mult).then_inc(acc_taken, 1)
                dve.wait_ge(acc_taken, t + 1)
                nc.vector.tensor_tensor(pre[:], mean_nb[:], row(s_sb, t), ALU.add).then_inc(pre_ready, 1)
                dve.wait_ge(pre_ready, t + 1)
                nc.vector.scalar_tensor_tensor(out=row(x_sb, t), in0=pre[:], scalar=0.0, in1=row(x_sb, t),
                                               op0=ALU.max, op1=ALU.add).then_inc(out_ready, 1)

            with dve.Fori(0, T // MASKS - 1) as turn:
                for k in range(MASKS):
                    finish(turn * MASKS + k, k % 2)
                    for slot in (2 * k, 2 * k + 1):
                        dve.wait_ge(raw_landed[slot], turn * 16 + 16)
                        to_mask(slot)
            for k in range(MASKS):
                finish(T - MASKS + k, k % 2)

        @block.tensor
        def _(pe):
            pe.wait_ge(weights_landed, 16 * WEIGHT_LOADS)
            for c in range(KC):
                for w_t, offset, where in ((wn_t, KC, 0), (ws_t, 0, D)):
                    for m in range(KC):
                        last = nc.tensor.matmul(ps_fold[c][:, where:where + D], w_t[:, m, c * P:(c + 1) * P],
                                                wc[:, offset + m, :], start=(m == 0), stop=(m == KC - 1))
            last.then_inc(folded, 1)
            pe.wait_ge(b_wide_ready, 1)
            for c in range(2 * KC):
                last = nc.tensor.matmul(ps_bias[:, 0:D], b_wide[:, c, :], wc[:, c, :],
                                        start=(c == 0), stop=(c == 2 * KC - 1))
            last.then_inc(bias_summed, 1)
            pe.wait_ge(ones_ready, 1)
            pe.wait_ge(abs_ready, 1)
            for c in range(KC):
                last = nc.tensor.matmul(ps_colsum[:, 0:D], ones[:], abs_wn[:, c, :],
                                        start=(c == 0), stop=(c == KC - 1))
            last.then_inc(colsum_ready, 1)
            pe.wait_ge(ident_ready, 1)

            def transpose_h(t, b):
                pe.wait_ge(h_ready, t + 1)
                for c in range(KC):
                    last = nc.tensor.transpose(ps_ht[b][:, c * P:(c + 1) * P], h[:, b, c * P:(c + 1) * P], ident[:])
                last.then_inc(ht_in_psum, 1)

            def products(t, b):
                pe.wait_ge(ht_ready, t + 1)
                for c in range(KC):
                    last = nc.tensor.matmul(ps_zs[b][:, :], h_t[:, b, c, :], w_fold[:, c, :],
                                            start=(c == 0), stop=(c == KC - 1))
                last.then_inc(zs_in_psum, 1)

            def project(turn):
                peeled = isinstance(turn, int)
                for k in range(BODY):
                    t = turn * BODY + k
                    if not peeled or k >= 2:
                        pe.wait_ge(ht_ready, t - 1)
                    transpose_h(t, k % 2)
                    if peeled and k == 1:
                        pe.wait_ge(w_ready, 1)
                    if not peeled or k >= 3:
                        pe.wait_ge(zs_taken, t - 2)
                    if not peeled or k >= 1:
                        products(t - 1, (k - 1) % 2)

            project(0)
            with pe.Fori(1, T // BODY) as turn:
                project(turn)
            pe.wait_ge(zs_taken, T - 2)
            products(T - 1, 1)
            pe.wait_ge(degree_ones_ready, 1)

            def sum_tile(t, k):
                peeled = isinstance(t, int)
                b = k % 2
                if not peeled or k >= 2:
                    pe.wait_ge(acc_taken, t - 1)
                for j in range(T):
                    if j % (T // 2) == 0:
                        pe.wait_ge(converted, t * 2 + (1 + j // (T // 2)))
                    if peeled and k == 0 and j >= T - GROUP:
                        pe.wait_ge(zs_taken, j + 1)
                    m = mask[:, k, j * P:(j + 1) * P]
                    if j < T - 1:
                        nc.tensor.matmul(acc[b][:, 0:DW], m, z_hi[:, j, :], start=(j == 0), stop=False)
                        nc.tensor.matmul(acc[b][:, 0:D], m, z_lo[:, j, :], start=False, stop=False)
                    else:
                        nc.tensor.matmul(acc[b][:, 0:D], m, z_lo[:, j, :], start=False, stop=False)
                        nc.tensor.matmul(acc[b][:, 0:DW], m, z_hi[:, j, :], start=False,
                                         stop=True).then_inc(tile_summed, 1)

            for k in range(MASKS):
                sum_tile(k, k)
            with pe.Fori(1, T // MASKS) as turn:
                for k in range(MASKS):
                    sum_tile(turn * MASKS + k, k)


def kernel(x, adj, L0_gnn_W_self, L0_gnn_b_self, L0_gnn_W_nb, L0_gnn_b_nb, L0_gnn_W_comb, L0_gnn_b_comb):
    import numpy as np
    import concourse.bacc as bacc
    from concourse.bass_utils import run_bass_kernel_spmd

    x, adj = np.asarray(x), np.asarray(adj)
    N, D = x.shape
    T, KC = N // P, D // P
    adj_t = adj.reshape(P, T, P, 2, T // 2).transpose(1, 3, 2, 4, 0).reshape(2 * T, P, N // 2)
    columns = [np.asarray(b).reshape(KC, P).T for b in (L0_gnn_b_self, L0_gnn_b_nb)]
    arrays = {
        "x": x,
        "adj_t": adj_t,
        "w_self_t": np.asarray(L0_gnn_W_self).T,
        "w_nb_t": np.asarray(L0_gnn_W_nb).T,
        "w_comb": np.asarray(L0_gnn_W_comb),
        "b_hidden": np.concatenate(columns, axis=1),
        "b_comb": np.asarray(L0_gnn_b_comb).reshape(1, D),
    }
    arrays = {name: np.ascontiguousarray(a) for name, a in arrays.items()}

    nc = bacc.Bacc("TRN2", target_bir_lowering=False, num_devices=1)
    ins = [nc.dram_tensor(name, a.shape, mybir.dt.from_np(a.dtype), kind="ExternalInput").ap()
           for name, a in arrays.items()]
    out = nc.dram_tensor("out", (N, D), F32, kind="ExternalOutput").ap()
    gnn_kernel(nc, *ins, out)
    return run_bass_kernel_spmd(nc, [arrays], core_ids=[0]).results[0]["out"]
```

```python
from contextlib import ExitStack

import concourse.bass as bass
from concourse import mybir

ALU = mybir.AluOpType
ACT = mybir.ActivationFunctionType
F32 = mybir.dt.float32
F16 = mybir.dt.float16
I32 = mybir.dt.int32

P = 128
EPS = 1e-5
LIMIT = 1024.0
MAGNITUDE = 0x7FFFFFFF
EXPONENT = 0x7F800000
INVERSE = 254 << 23
TINY = 1e-30

GROUP = 4
BODY = 8
LEVELS = 5
MASKS = 4
RAWS = 2 * MASKS
Z_BANKS = 4
WARM_UP = 10


def gnn_kernel(nc, x, adj_t, w_self_t, w_nb_t, w_comb, b_hidden, b_comb, out):
    N, D = x.shape
    T = N // P
    KC = D // P
    HALF = T * P // 2

    x_dram = x.rearrange("(p t) d -> p t d", p=P)
    out_dram = out.rearrange("(p t) d -> p t d", p=P)

    with ExitStack() as ctx:
        def sb(name, shape, dt):
            return ctx.enter_context(nc.sbuf_tensor(name, shape, dt))

        def psum(name, shape, dt):
            return ctx.enter_context(nc.psum_tensor(name, shape, dt))

        def sem(name):
            return ctx.enter_context(nc.semaphore(name))

        x_sb = sb("x_sb", [P, T, D], F32)
        s_sb = sb("s_sb", [P, T, D], F32)
        z = sb("z", [P, T, 2 * D], F16)
        raw = sb("raw", [P, RAWS, HALF], I32)
        mask = sb("mask", [P, MASKS, 2 * HALF], F16)
        mask_halves = mask[:, :, :].rearrange("p s (e n) -> p (s e) n", e=2)
        w_fold = sb("w_fold", [P, KC, 2 * D], F32)
        unscale = sb("unscale", [P, D], F32)
        bias = sb("bias", [P, D], F32)
        ident = sb("ident", [P, P], F32)
        ones = sb("ones", [P, P], F32)
        ones_column = sb("ones_column", [P, 1], F16)
        h_space = sb("h_space", [P, 4, D], F32)
        h = h_space[:, 0:2, :]
        h_t = h_space[:, 2:4, :].rearrange("p b (c n) -> p b c n", c=KC)
        block_sums = h_space[:, :, :].rearrange("p b n -> p (b n)").bitcast(F16)
        counts = sb("counts", [P, 2, P], F16)
        moments = sb("moments", [P, GROUP, 6], F32)
        mean_sum = sb("mean_sum", [P, GROUP], F32)
        mean_gap = sb("mean_gap", [P, GROUP], F32)
        square_sum = sb("square_sum", [P, GROUP], F32)
        within = sb("within", [P, GROUP], F32)
        between = sb("between", [P, GROUP], F32)
        var_eps = sb("var_eps", [P, GROUP], F32)
        std = sb("std", [P, GROUP], F32)
        r0 = sb("r0", [P, GROUP], F32)
        newton_a = sb("newton_a", [P, GROUP], F32)
        newton_b = sb("newton_b", [P, GROUP], F32)
        rstd = sb("rstd", [P, 2, GROUP], F32)
        shift = sb("shift", [P, 2, GROUP], F32)
        deg = sb("deg", [P, 1], F32)
        rdeg = sb("rdeg", [P, 1], F32)
        low_sum = sb("low_sum", [P, D], F32)
        whole_sum = sb("whole_sum", [P, D], F32)
        pre = sb("pre", [P, D], F32)
        b_cols = sb("b_cols", [P, 2 * KC], F32)

        w_stage = mask[:, MASKS - 1, :].bitcast(F32)
        ws_t = w_stage[:, 0:KC * D].rearrange("p (c n) -> p c n", c=KC)
        wn_t = w_stage[:, KC * D:2 * KC * D].rearrange("p (c n) -> p c n", c=KC)
        wc = w_stage[:, 2 * KC * D:4 * KC * D].rearrange("p (c n) -> p c n", c=2 * KC)
        stage2 = mask[:, MASKS - 2, :].bitcast(F32)
        abs_wn = stage2[:, 0:KC * D].rearrange("p (c n) -> p c n", c=KC)
        b_wide = stage2[:, KC * D:KC * D + 2 * KC * P].rearrange("p (c n) -> p c n", c=2 * KC)
        b_comb_bc = stage2[:, 5 * D:6 * D]
        share = stage2[:, 6 * D:7 * D]
        rescale = stage2[:, 7 * D:8 * D]

        acc = [psum(f"acc{i}", [P, 512], F32) for i in range(2)]
        ps_ht = [psum(f"ps_ht{i}", [P, 512], F32) for i in range(2)]
        ps_zs = [psum(f"ps_zs{i}", [P, 512], F32) for i in range(Z_BANKS)]
        ps_wn, ps_ws = ps_zs[0:KC], ps_zs[KC:2 * KC]
        ps_colsum, ps_bias = acc
        ps_deg = ps_ht

        x_landed = [sem(f"x_landed{i}") for i in range(2)]
        wn_landed = sem("wn_landed")
        ws_landed = sem("ws_landed")
        biases_landed = sem("biases_landed")
        early_landed = [sem(f"early_landed{i}") for i in range(2)]
        raw_landed = [sem(f"raw_landed{i}") for i in range(RAWS)]
        ident_zero = sem("ident_zero")
        ident_ready = sem("ident_ready")
        ones_ready = sem("ones_ready")
        b_wide_ready = sem("b_wide_ready")
        wn_folded = sem("wn_folded")
        ws_folded = sem("ws_folded")
        ws_ready = sem("ws_ready")
        abs_ready = sem("abs_ready")
        colsum_ready = sem("colsum_ready")
        share_ready = sem("share_ready")
        unscale_ready = sem("unscale_ready")
        rescale_ready = sem("rescale_ready")
        bias_summed = sem("bias_summed")
        bias_ready = sem("bias_ready")
        wn_ready = sem("wn_ready")
        moments_ready = sem("moments_ready")
        sums_ready = sem("sums_ready")
        parts_ready = sem("parts_ready")
        var_ready = sem("var_ready")
        std_ready = sem("std_ready")
        r0_ready = sem("r0_ready")
        newton_a_ready = sem("newton_a_ready")
        newton_b_ready = sem("newton_b_ready")
        rstd_ready = sem("rstd_ready")
        shift_ready = sem("shift_ready")
        h_ready = sem("h_ready")
        ht_in_psum = sem("ht_in_psum")
        ht_ready = sem("ht_ready")
        zs_in_psum = sem("zs_in_psum")
        zs_copied = sem("zs_copied")
        zs_taken = sem("zs_taken")
        bias_added = sem("bias_added")
        converted = sem("converted")
        tile_summed = sem("tile_summed")
        counts_step = [sem(f"counts_step{i}") for i in range(LEVELS)]
        deg_ready = sem("deg_ready")
        rdeg_ready = sem("rdeg_ready")
        low_sum_ready = sem("low_sum_ready")
        whole_sum_ready = sem("whole_sum_ready")
        scaled_ready = sem("scaled_ready")
        pre_ready = sem("pre_ready")
        relu_ready = sem("relu_ready")
        out_ready = sem("out_ready")
        stored = sem("stored")

        def row(tensor, t):
            if isinstance(t, int):
                return tensor[:, t, :]
            return tensor[:, bass.ds(t, 1), :].rearrange("p a n -> p (a n)")

        block = ctx.enter_context(nc.Block())

        @block.sync
        def _(sp):
            def load_x(group):
                tiles = slice(group * GROUP, (group + 1) * GROUP)
                sp.dma_start(x_sb[:, tiles, :], x_dram[:, tiles, :]).then_inc(x_landed[group % 2], 16)

            wc_dram = w_comb.rearrange("(c p) n -> p c n", p=P)
            sp.dma_start(wn_t, w_nb_t.rearrange("(c p) n -> p c n", p=P)).then_inc(wn_landed, 16)
            sp.dma_start(wc[:, KC:2 * KC, :], wc_dram[:, KC:2 * KC, :]).then_inc(wn_landed, 16)
            load_x(0)
            sp.dma_start(b_cols[:, :], b_hidden).then_inc(biases_landed, 16)
            sp.dma_start(b_comb_bc, b_comb.broadcast_to([P, D])).then_inc(biases_landed, 16)
            sp.dma_start(ws_t, w_self_t.rearrange("(c p) n -> p c n", p=P)).then_inc(ws_landed, 16)
            sp.dma_start(wc[:, 0:KC, :], wc_dram[:, 0:KC, :]).then_inc(ws_landed, 16)
            load_x(1)
            for group in range(2, T // GROUP):
                sp.wait_ge(x_landed[group % 2], 16 * (group // 2))
                load_x(group)
            for half in range(RAWS):
                if half >= 2:
                    sp.wait_ge(early_landed[half % 2], 16 * (half // 2))
                sp.dma_start(raw[:, half, :], adj_t[half]).then_inc(early_landed[half % 2], 16)
            with sp.Fori(1, T // MASKS) as turn:
                for slot in range(RAWS):
                    sp.wait_ge(converted, turn * RAWS + (slot + 1 - RAWS))
                    sp.dma_start(raw[:, slot, :],
                                 adj_t[bass.ds(turn * RAWS + slot, 1)].rearrange("a p n -> p (a n)")
                                 ).then_inc(raw_landed[slot], 16)

        @block.gpsimd
        def _(pool):
            nc.gpsimd.memset(ident[:], 0.0).then_inc(ident_zero, 1)
            pool.wait_ge(ident_zero, 1)
            nc.gpsimd.affine_select(out=ident[:], in_=ident[:], compare_op=ALU.not_equal, fill=1.0, base=0,
                                    pattern=[[-1, P]], channel_multiplier=1).then_inc(ident_ready, 1)
            pool.wait_ge(ones_ready, 1)
            pool.wait_ge(biases_landed, 2 * 16)
            for c in range(2 * KC):
                last = nc.gpsimd.tensor_scalar(b_wide[:, c, :], ones[:], b_cols[:, c:c + 1], None, ALU.mult)
            last.then_inc(b_wide_ready, 1)
            pool.wait_ge(bias_ready, 1)

            def add_bias(t):
                pool.wait_ge(zs_copied, t + 1)
                nc.gpsimd.tensor_tensor(row(s_sb, t), row(s_sb, t), bias[:], ALU.add).then_inc(bias_added, 1)

            with pool.Fori(0, T) as t:
                add_bias(t)

            pool.wait_ge(bias_added, T)
            with pool.Fori(0, T) as t:
                pool.wait_ge(scaled_ready, t + 1)
                nc.gpsimd.tensor_tensor(pre[:], pre[:], row(s_sb, t), ALU.add).then_inc(pre_ready, 1)
                pool.wait_ge(relu_ready, t + 1)
                nc.gpsimd.tensor_tensor(row(x_sb, t), row(x_sb, t), pre[:], ALU.add).then_inc(out_ready, 1)

        @block.scalar
        def _(act):
            def normalise(t, k):
                pair, q = k // GROUP, k % GROUP
                nc.scalar.activation(h[:, k % 2, :], row(x_sb, t), ACT.Relu, bias=shift[:, pair, q:q + 1],
                                     scale=rstd[:, pair, q:q + 1]).then_inc(h_ready, 1)

            def take_ht(t, b):
                act.wait_ge(ht_in_psum, t + 1)
                nc.scalar.copy(h_t[:, b].rearrange("p c n -> p (c n)"), ps_ht[b][:, 0:D]).then_inc(ht_ready, 1)

            def copy_zs(t, b):
                act.wait_ge(zs_in_psum, t + 1)
                nc.scalar.copy(row(z, t)[:, 0:D], ps_zs[b][:, 0:D])
                nc.scalar.copy(row(s_sb, t), ps_zs[b][:, D:2 * D]).then_inc(zs_copied, 1)

            def deviation(group):
                act.wait_ge(var_ready, group + 1)
                nc.scalar.activation(std[:], var_eps[:], ACT.Sqrt).then_inc(std_ready, 1)

            def step(t, k):
                first = T if not isinstance(t, int) else t
                if k % GROUP == 0:
                    act.wait_ge(shift_ready, t + GROUP)
                if first >= 2:
                    act.wait_ge(ht_in_psum, t - 1)
                normalise(t, k)
                if first >= 3:
                    act.wait_ge(zs_in_psum, t - 2)
                if first >= 1:
                    take_ht(t - 1, (k - 1) % 2)
                if first >= 2:
                    copy_zs(t - 2, (k - 2) % Z_BANKS)

            deviation(0)
            step(0, 0)
            act.wait_ge(ws_folded, 1)
            for c in range(KC):
                last = nc.scalar.copy(w_fold[:, c, D:2 * D], ps_ws[c][:, 0:D])
            last.then_inc(ws_ready, 1)
            step(1, 1)
            step(2, 2)
            deviation(1)
            for t in range(3, BODY - 1):
                step(t, t)
            with act.Fori(1, T // BODY) as turn:
                deviation(turn * 2)
                step(turn * BODY - 1, BODY - 1)
                for k in range(0, 3):
                    step(turn * BODY + k, k)
                deviation(turn * 2 + 1)
                for k in range(3, BODY - 1):
                    step(turn * BODY + k, k)
            step(T - 1, BODY - 1)
            act.wait_ge(zs_in_psum, T - 2)
            take_ht(T - 1, 1)
            copy_zs(T - 2, (T - 2) % Z_BANKS)
            copy_zs(T - 1, (T - 1) % Z_BANKS)

            def finish(t, b):
                act.wait_ge(tile_summed, t + 1)
                nc.scalar.copy(low_sum[:], acc[b][:, D:2 * D]).then_inc(low_sum_ready, 1)
                act.wait_ge(pre_ready, t + 1)
                nc.scalar.activation(pre[:], pre[:], ACT.Relu).then_inc(relu_ready, 1)

            with act.Fori(0, T // MASKS - 1) as turn:
                for k in range(MASKS):
                    finish(turn * MASKS + k, k % 2)
                act.wait_ge(out_ready, (turn + 1) * MASKS)
                act.dma_start(out_dram[:, bass.ds(turn * MASKS, MASKS), :],
                              x_sb[:, bass.ds(turn * MASKS, MASKS), :]).then_inc(stored, 16)
            for t in range(T - MASKS, T):
                finish(t, t % 2)
                act.wait_ge(out_ready, t + 1)
                act.dma_start(out_dram[:, t, :], x_sb[:, t, :]).then_inc(stored, 16)
            act.wait_ge(stored, 16 * (T // MASKS - 1 + MASKS))

        @block.vector
        def _(dve):
            def variance(group):
                for q in range(GROUP):
                    last = nc.vector.bn_stats(moments[:, q, :], row(x_sb, group * GROUP + q))
                last.then_inc(moments_ready, 1)
                dve.wait_ge(moments_ready, group + 1)
                nc.vector.tensor_tensor(mean_sum[:], moments[:, :, 1], moments[:, :, 4], ALU.add)
                nc.vector.tensor_tensor(mean_gap[:], moments[:, :, 1], moments[:, :, 4], ALU.subtract)
                nc.vector.tensor_tensor(square_sum[:], moments[:, :, 2], moments[:, :, 5],
                                        ALU.add).then_inc(sums_ready, 1)
                dve.wait_ge(sums_ready, group + 1)
                nc.vector.tensor_scalar(within[:], square_sum[:], 1.0 / D, EPS, ALU.mult, ALU.add)
                nc.vector.scalar_tensor_tensor(out=between[:], in0=mean_gap[:], scalar=0.25, in1=mean_gap[:],
                                               op0=ALU.mult, op1=ALU.mult).then_inc(parts_ready, 1)
                dve.wait_ge(parts_ready, group + 1)
                nc.vector.tensor_tensor(var_eps[:], within[:], between[:], ALU.add).then_inc(var_ready, 1)

            def normaliser(group, pair, peeled):
                dve.wait_ge(std_ready, group + 1)
                nc.vector.reciprocal(r0[:], std[:]).then_inc(r0_ready, 1)
                dve.wait_ge(r0_ready, group + 1)
                nc.vector.tensor_tensor(newton_a[:], var_eps[:], r0[:], ALU.mult).then_inc(newton_a_ready, 1)
                dve.wait_ge(newton_a_ready, group + 1)
                nc.vector.scalar_tensor_tensor(out=newton_b[:], in0=newton_a[:], scalar=-0.5, in1=r0[:],
                                               op0=ALU.mult, op1=ALU.mult).then_inc(newton_b_ready, 1)
                dve.wait_ge(newton_b_ready, group + 1)
                if not peeled:
                    dve.wait_ge(h_ready, (group - 1) * GROUP)
                nc.vector.scalar_tensor_tensor(out=rstd[:, pair, :], in0=newton_b[:], scalar=1.5, in1=r0[:],
                                               op0=ALU.add, op1=ALU.mult).then_inc(rstd_ready, 1)
                dve.wait_ge(rstd_ready, group + 1)
                nc.vector.scalar_tensor_tensor(out=shift[:, pair, :], in0=mean_sum[:], scalar=-0.5,
                                               in1=rstd[:, pair, :], op0=ALU.mult,
                                               op1=ALU.mult).then_inc(shift_ready, GROUP)

            def low_part(t, b):
                dve.wait_ge(zs_copied, t + 1)
                nc.vector.tensor_tensor(row(z, t)[:, D:2 * D], ps_zs[b][:, 0:D], row(z, t)[:, 0:D],
                                        ALU.subtract).then_inc(zs_taken, 1)

            def to_mask(half):
                nc.vector.tensor_scalar(row(mask_halves, half), row(raw, half), 0, None,
                                        ALU.is_gt).then_inc(converted, 1)

            nc.vector.memset(ones_column[:], 1.0)
            nc.vector.memset(ones[:], 1.0).then_inc(ones_ready, 1)
            dve.wait_ge(x_landed[0], 16)
            variance(0)
            dve.wait_ge(wn_folded, 1)
            for c in range(KC):
                last = nc.vector.tensor_scalar(abs_wn[:, c, :].bitcast(I32), ps_wn[c][:, 0:D].bitcast(I32),
                                               MAGNITUDE, None, ALU.bitwise_and)
            last.then_inc(abs_ready, 1)
            normaliser(0, 0, True)
            dve.wait_ge(colsum_ready, 1)
            nc.vector.tensor_scalar(share, ps_colsum[:, 0:D], TINY, 1.0 / LIMIT,
                                    ALU.max, ALU.mult).then_inc(share_ready, 1)
            dve.wait_ge(share_ready, 1)
            nc.vector.tensor_scalar(unscale[:].bitcast(I32), share.bitcast(I32), EXPONENT, None,
                                    ALU.bitwise_and).then_inc(unscale_ready, 1)
            dve.wait_ge(unscale_ready, 1)
            nc.vector.tensor_scalar(rescale.bitcast(I32), unscale[:].bitcast(I32), -1.0, float(INVERSE),
                                    ALU.mult, ALU.add).then_inc(rescale_ready, 1)
            dve.wait_ge(rescale_ready, 1)
            for c in range(KC):
                last = nc.vector.tensor_tensor(w_fold[:, c, 0:D], ps_wn[c][:, 0:D], rescale, ALU.mult)
            last.then_inc(wn_ready, 1)
            dve.wait_ge(bias_summed, 1)
            nc.vector.tensor_tensor(bias[:], ps_bias[:, 0:D], b_comb_bc, ALU.add).then_inc(bias_ready, 1)
            dve.wait_ge(x_landed[1], 16)
            variance(1)
            normaliser(1, 1, True)
            for t in range(0, GROUP - 1):
                low_part(t, t % Z_BANKS)
            dve.wait_ge(early_landed[0], 16)
            to_mask(0)
            with dve.Fori(1, T // BODY) as turn:
                dve.wait_ge(x_landed[0], turn * 16 + 16)
                variance(turn * 2)
                normaliser(turn * 2, 0, False)
                dve.wait_ge(early_landed[1], turn * 16)
                to_mask(turn * 2 - 1)
                for t in range(-GROUP - 1, -1):
                    low_part(turn * BODY + t, t % Z_BANKS)
                dve.wait_ge(x_landed[1], turn * 16 + 16)
                variance(turn * 2 + 1)
                normaliser(turn * 2 + 1, 1, False)
                dve.wait_ge(early_landed[0], turn * 16 + 16)
                to_mask(turn * 2)
                for t in range(-1, GROUP - 1):
                    low_part(turn * BODY + t, t % Z_BANKS)
            for t in range(T - GROUP - 1, T):
                low_part(t, t % Z_BANKS)
            dve.wait_ge(early_landed[1], 16 * RAWS // 2)
            to_mask(RAWS - 1)

            def count(t, k):
                for level in range(LEVELS):
                    width = HALF >> level
                    if level == 0:
                        left, right = mask[:, k, 0:HALF], mask[:, k, HALF:2 * HALF]
                    else:
                        dve.wait_ge(counts_step[level - 1], t + 1)
                        left, right = block_sums[:, 0:width], block_sums[:, width:2 * width]
                    target = block_sums[:, 0:width] if level < LEVELS - 1 else counts[:, k % 2, :]
                    nc.vector.tensor_tensor(target, left, right, ALU.add).then_inc(counts_step[level], 1)

            def finish(t, b):
                dve.wait_ge(tile_summed, t + 1)
                nc.vector.tensor_scalar(deg[:], ps_deg[b][:, 0:1], 1.0, None, ALU.max).then_inc(deg_ready, 1)
                dve.wait_ge(low_sum_ready, t + 1)
                nc.vector.tensor_tensor(whole_sum[:], acc[b][:, 0:D], low_sum[:], ALU.add).then_inc(whole_sum_ready, 1)
                dve.wait_ge(deg_ready, t + 1)
                nc.vector.reciprocal(rdeg[:], deg[:]).then_inc(rdeg_ready, 1)
                dve.wait_ge(rdeg_ready, t + 1)
                dve.wait_ge(whole_sum_ready, t + 1)
                if not isinstance(t, int) or t > 0:
                    dve.wait_ge(out_ready, t)
                nc.vector.scalar_tensor_tensor(out=pre[:], in0=whole_sum[:], scalar=rdeg[:], in1=unscale[:],
                                               op0=ALU.mult, op1=ALU.mult).then_inc(scaled_ready, 1)

            def replace(turn, k):
                for slot in (2 * k, 2 * k + 1):
                    dve.wait_ge(raw_landed[slot], turn * 16 + 16)
                    to_mask(slot)

            def main_turn(turn, last):
                for k in range(MASKS):
                    t = turn * MASKS + k
                    count(t, k)
                    finish(t, k % 2)
                    if not last:
                        replace(turn, k)

            main_turn(0, False)
            with dve.Fori(1, T // MASKS - 1) as turn:
                main_turn(turn, False)
            main_turn(T // MASKS - 1, True)

        @block.tensor
        def _(pe):
            pe.wait_ge(ones_ready, 1)
            for _ in range(WARM_UP):
                nc.tensor.matmul(ps_bias[:, 0:P], ones[:], ones[:], start=True, stop=True)

            def fold(w_t, offset, target, c):
                for m in range(KC):
                    last = nc.tensor.matmul(target[c][:, 0:D], w_t[:, m, c * P:(c + 1) * P], wc[:, offset + m, :],
                                            start=(m == 0), stop=(m == KC - 1))
                return last

            pe.wait_ge(wn_landed, 2 * 16)
            for c in range(KC):
                last = fold(wn_t, KC, ps_wn, c)
            last.then_inc(wn_folded, 1)
            pe.wait_ge(ws_landed, 2 * 16)
            fold(ws_t, 0, ps_ws, 0)
            pe.wait_ge(abs_ready, 1)
            for c in range(KC):
                last = nc.tensor.matmul(ps_colsum[:, 0:D], ones[:], abs_wn[:, c, :],
                                        start=(c == 0), stop=(c == KC - 1))
            last.then_inc(colsum_ready, 1)
            fold(ws_t, 0, ps_ws, 1).then_inc(ws_folded, 1)
            pe.wait_ge(b_wide_ready, 1)
            for c in range(2 * KC):
                last = nc.tensor.matmul(ps_bias[:, 0:D], b_wide[:, c, :], wc[:, c, :],
                                        start=(c == 0), stop=(c == 2 * KC - 1))
            last.then_inc(bias_summed, 1)
            pe.wait_ge(ident_ready, 1)

            def transpose_h(t, b):
                pe.wait_ge(h_ready, t + 1)
                for c in range(KC):
                    last = nc.tensor.transpose(ps_ht[b][:, c * P:(c + 1) * P], h[:, b, c * P:(c + 1) * P], ident[:])
                last.then_inc(ht_in_psum, 1)

            def products(t, b, bank):
                pe.wait_ge(ht_ready, t + 1)
                for c in range(KC):
                    last = nc.tensor.matmul(ps_zs[bank][:, :], h_t[:, b, c, :], w_fold[:, c, :],
                                            start=(c == 0), stop=(c == KC - 1))
                last.then_inc(zs_in_psum, 1)

            def project(turn):
                peeled = isinstance(turn, int)
                for k in range(BODY):
                    t = turn * BODY + k
                    if not peeled or k >= 2:
                        pe.wait_ge(ht_ready, t - 1)
                    transpose_h(t, k % 2)
                    if peeled and k == 1:
                        pe.wait_ge(wn_ready, 1)
                        pe.wait_ge(ws_ready, 1)
                    if not peeled or k > Z_BANKS:
                        pe.wait_ge(zs_taken, t - Z_BANKS)
                    if not peeled or k >= 1:
                        products(t - 1, (k - 1) % 2, (k - 1) % Z_BANKS)

            project(0)
            with pe.Fori(1, T // BODY) as turn:
                project(turn)
            pe.wait_ge(zs_taken, T - Z_BANKS)
            products(T - 1, 1, (T - 1) % Z_BANKS)

            def sum_tile(t, k):
                peeled = isinstance(t, int)
                b = k % 2
                if not peeled or k >= 2:
                    pe.wait_ge(scaled_ready, t - 1)
                for j in range(T):
                    if j % (T // 2) == 0:
                        pe.wait_ge(converted, t * 2 + (1 + j // (T // 2)))
                    if peeled and k == 0 and j >= T - GROUP - 1:
                        pe.wait_ge(zs_taken, j + 1)
                    last = nc.tensor.matmul(acc[b][:, :], mask[:, k, j * P:(j + 1) * P], z[:, j, :],
                                            start=(j == 0), stop=(j == T - 1))
                pe.wait_ge(counts_step[LEVELS - 1], t + 1)
                nc.tensor.matmul(ps_deg[b][:, 0:1], counts[:, b, :], ones_column[:],
                                 start=True, stop=True).then_inc(tile_summed, 1)

            for k in range(MASKS):
                sum_tile(k, k)
            with pe.Fori(1, T // MASKS) as turn:
                for k in range(MASKS):
                    sum_tile(turn * MASKS + k, k)


def kernel(x, adj, L0_gnn_W_self, L0_gnn_b_self, L0_gnn_W_nb, L0_gnn_b_nb, L0_gnn_W_comb, L0_gnn_b_comb):
    import numpy as np
    import concourse.bacc as bacc
    from concourse.bass_utils import run_bass_kernel_spmd

    x, adj = np.asarray(x), np.asarray(adj)
    N, D = x.shape
    T, KC = N // P, D // P
    adj_t = adj.reshape(P, T, P, 2, T // 2).transpose(1, 3, 2, 4, 0).reshape(2 * T, P, N // 2)
    columns = [np.asarray(b).reshape(KC, P).T for b in (L0_gnn_b_self, L0_gnn_b_nb)]
    arrays = {
        "x": x,
        "adj_t": adj_t,
        "w_self_t": np.asarray(L0_gnn_W_self).T,
        "w_nb_t": np.asarray(L0_gnn_W_nb).T,
        "w_comb": np.asarray(L0_gnn_W_comb),
        "b_hidden": np.concatenate(columns, axis=1),
        "b_comb": np.asarray(L0_gnn_b_comb).reshape(1, D),
    }
    arrays = {name: np.ascontiguousarray(a) for name, a in arrays.items()}

    nc = bacc.Bacc("TRN2", target_bir_lowering=False, num_devices=1)
    ins = [nc.dram_tensor(name, a.shape, mybir.dt.from_np(a.dtype), kind="ExternalInput").ap()
           for name, a in arrays.items()]
    out = nc.dram_tensor("out", (N, D), F32, kind="ExternalOutput").ap()
    gnn_kernel(nc, *ins, out)
    return run_bass_kernel_spmd(nc, [arrays], core_ids=[0]).results[0]["out"]
```

```python
from contextlib import ExitStack

import concourse.bass as bass
from concourse import mybir

ALU = mybir.AluOpType
ACT = mybir.ActivationFunctionType
F32 = mybir.dt.float32
F16 = mybir.dt.float16
I32 = mybir.dt.int32

P = 128
EPS = 1e-5
LIMIT = 1024.0
MAGNITUDE = 0x7FFFFFFF
EXPONENT = 0x7F800000
INVERSE = 254 << 23
TINY = 1e-30

GROUP = 4
BODY = 8
LEVELS = 5
MASKS = 4
RAWS = 2 * MASKS
STEEP = 32.0
Z_BANKS = 4
WARM_UP = 10


def gnn_kernel(nc, x, adj_t, w_self_t, w_nb_t, w_comb, b_hidden, b_comb, out):
    N, D = x.shape
    T = N // P
    KC = D // P
    HALF = T * P // 2

    x_dram = x.rearrange("(p t) d -> p t d", p=P)
    out_dram = out.rearrange("(p t) d -> p t d", p=P)

    with ExitStack() as ctx:
        def sb(name, shape, dt):
            return ctx.enter_context(nc.sbuf_tensor(name, shape, dt))

        def psum(name, shape, dt):
            return ctx.enter_context(nc.psum_tensor(name, shape, dt))

        def sem(name):
            return ctx.enter_context(nc.semaphore(name))

        x_sb = sb("x_sb", [P, T, D], F32)
        s_sb = sb("s_sb", [P, T, D], F32)
        z = sb("z", [P, T, 2 * D], F16)
        raw = sb("raw", [P, RAWS, HALF], I32)
        mask = sb("mask", [P, MASKS, 2 * HALF], F16)
        mask_halves = mask[:, :, :].rearrange("p s (e n) -> p (s e) n", e=2)
        w_fold = sb("w_fold", [P, KC, 2 * D], F32)
        unscale = sb("unscale", [P, D], F32)
        bias = sb("bias", [P, D], F32)
        ident = sb("ident", [P, P], F32)
        ones = sb("ones", [P, P], F32)
        ones_column = sb("ones_column", [P, 1], F16)
        h_space = sb("h_space", [P, 4, D], F32)
        h = h_space[:, 0:2, :]
        h_t = h_space[:, 2:4, :].rearrange("p b (c n) -> p b c n", c=KC)
        block_sums = h_space[:, :, :].rearrange("p b n -> p (b n)").bitcast(F16)
        counts = sb("counts", [P, 2, P], F16)
        low_sum, whole_sum = w_fold[:, 0, 0:D], w_fold[:, 0, D:2 * D]
        scaled, pre = w_fold[:, 1, 0:D], w_fold[:, 1, D:2 * D]
        moments = sb("moments", [P, GROUP, 6], F32)
        mean_sum = sb("mean_sum", [P, GROUP], F32)
        mean_gap = sb("mean_gap", [P, GROUP], F32)
        square_sum = sb("square_sum", [P, GROUP], F32)
        within = sb("within", [P, GROUP], F32)
        between = sb("between", [P, GROUP], F32)
        var_eps = sb("var_eps", [P, GROUP], F32)
        std = sb("std", [P, GROUP], F32)
        r0 = sb("r0", [P, GROUP], F32)
        newton_a = sb("newton_a", [P, GROUP], F32)
        newton_b = sb("newton_b", [P, GROUP], F32)
        rstd = sb("rstd", [P, 2, GROUP], F32)
        shift = sb("shift", [P, 2, GROUP], F32)
        deg = sb("deg", [P, 1], F32)
        rdeg = sb("rdeg", [P, 1], F32)
        steep_bias = sb("steep_bias", [P, 1], F32)
        b_cols = sb("b_cols", [P, 2 * KC], F32)

        w_stage = mask[:, MASKS - 1, :].bitcast(F32)
        ws_t = w_stage[:, 0:KC * D].rearrange("p (c n) -> p c n", c=KC)
        wn_t = w_stage[:, KC * D:2 * KC * D].rearrange("p (c n) -> p c n", c=KC)
        wc = w_stage[:, 2 * KC * D:4 * KC * D].rearrange("p (c n) -> p c n", c=2 * KC)
        stage2 = mask[:, MASKS - 2, :].bitcast(F32)
        abs_wn = stage2[:, 0:KC * D].rearrange("p (c n) -> p c n", c=KC)
        b_wide = stage2[:, KC * D:KC * D + 2 * KC * P].rearrange("p (c n) -> p c n", c=2 * KC)
        b_comb_bc = stage2[:, 5 * D:6 * D]
        share = stage2[:, 6 * D:7 * D]
        rescale = stage2[:, 7 * D:8 * D]

        acc = [psum(f"acc{i}", [P, 512], F32) for i in range(2)]
        ps_ht = [psum(f"ps_ht{i}", [P, 512], F32) for i in range(2)]
        ps_zs = [psum(f"ps_zs{i}", [P, 512], F32) for i in range(Z_BANKS)]
        ps_wn, ps_ws = ps_zs[0:KC], ps_zs[KC:2 * KC]
        ps_colsum, ps_bias = acc
        ps_deg = ps_ht

        x_landed = [sem(f"x_landed{i}") for i in range(2)]
        wn_landed = sem("wn_landed")
        ws_landed = sem("ws_landed")
        biases_landed = sem("biases_landed")
        early_landed = [sem(f"early_landed{i}") for i in range(2)]
        raw_landed = [sem(f"raw_landed{i}") for i in range(RAWS)]
        steep_bias_ready = sem("steep_bias_ready")
        ident_zero = sem("ident_zero")
        ident_ready = sem("ident_ready")
        ones_ready = sem("ones_ready")
        b_wide_ready = sem("b_wide_ready")
        wn_folded = sem("wn_folded")
        ws_folded = sem("ws_folded")
        ws_ready = sem("ws_ready")
        abs_ready = sem("abs_ready")
        colsum_ready = sem("colsum_ready")
        share_ready = sem("share_ready")
        unscale_ready = sem("unscale_ready")
        rescale_ready = sem("rescale_ready")
        bias_summed = sem("bias_summed")
        bias_ready = sem("bias_ready")
        wn_ready = sem("wn_ready")
        moments_ready = sem("moments_ready")
        sums_ready = sem("sums_ready")
        parts_ready = sem("parts_ready")
        var_ready = sem("var_ready")
        std_ready = sem("std_ready")
        r0_ready = sem("r0_ready")
        newton_a_ready = sem("newton_a_ready")
        newton_b_ready = sem("newton_b_ready")
        rstd_ready = sem("rstd_ready")
        shift_ready = sem("shift_ready")
        h_ready = sem("h_ready")
        ht_in_psum = sem("ht_in_psum")
        ht_ready = sem("ht_ready")
        zs_in_psum = sem("zs_in_psum")
        zs_copied = sem("zs_copied")
        zs_taken = sem("zs_taken")
        bias_added = sem("bias_added")
        converted = sem("converted")
        tile_summed = sem("tile_summed")
        deg_summed = sem("deg_summed")
        counts_step = [sem(f"counts_step{i}") for i in range(LEVELS)]
        deg_ready = sem("deg_ready")
        rdeg_ready = sem("rdeg_ready")
        low_sum_ready = sem("low_sum_ready")
        whole_sum_ready = sem("whole_sum_ready")
        scaled_ready = sem("scaled_ready")
        pre_ready = sem("pre_ready")
        out_ready = sem("out_ready")
        stored = sem("stored")

        def row(tensor, t):
            if isinstance(t, int):
                return tensor[:, t, :]
            return tensor[:, bass.ds(t, 1), :].rearrange("p a n -> p (a n)")

        block = ctx.enter_context(nc.Block())

        @block.sync
        def _(sp):
            def load_x(group):
                tiles = slice(group * GROUP, (group + 1) * GROUP)
                sp.dma_start(x_sb[:, tiles, :], x_dram[:, tiles, :]).then_inc(x_landed[group % 2], 16)

            wc_dram = w_comb.rearrange("(c p) n -> p c n", p=P)
            load_x(0)
            sp.dma_start(wn_t, w_nb_t.rearrange("(c p) n -> p c n", p=P)).then_inc(wn_landed, 16)
            sp.dma_start(wc[:, KC:2 * KC, :], wc_dram[:, KC:2 * KC, :]).then_inc(wn_landed, 16)
            sp.dma_start(b_cols[:, :], b_hidden).then_inc(biases_landed, 16)
            sp.dma_start(b_comb_bc, b_comb.broadcast_to([P, D])).then_inc(biases_landed, 16)
            sp.dma_start(ws_t, w_self_t.rearrange("(c p) n -> p c n", p=P)).then_inc(ws_landed, 16)
            sp.dma_start(wc[:, 0:KC, :], wc_dram[:, 0:KC, :]).then_inc(ws_landed, 16)
            load_x(1)
            for group in range(2, T // GROUP):
                sp.wait_ge(x_landed[group % 2], 16 * (group // 2))
                load_x(group)
            for half in range(RAWS):
                if half >= 2:
                    sp.wait_ge(early_landed[half % 2], 16 * (half // 2))
                sp.dma_start(raw[:, half, :], adj_t[half]).then_inc(early_landed[half % 2], 16)
            with sp.Fori(1, T // MASKS) as turn:
                for slot in range(RAWS):
                    sp.wait_ge(converted, turn * RAWS + (slot + 1 - RAWS))
                    sp.dma_start(raw[:, slot, :],
                                 adj_t[bass.ds(turn * RAWS + slot, 1)].rearrange("a p n -> p (a n)")
                                 ).then_inc(raw_landed[slot], 16)

        @block.gpsimd
        def _(pool):
            nc.gpsimd.memset(steep_bias[:], -STEEP).then_inc(steep_bias_ready, 1)
            nc.gpsimd.memset(ident[:], 0.0).then_inc(ident_zero, 1)
            pool.wait_ge(ident_zero, 1)
            nc.gpsimd.affine_select(out=ident[:], in_=ident[:], compare_op=ALU.not_equal, fill=1.0, base=0,
                                    pattern=[[-1, P]], channel_multiplier=1).then_inc(ident_ready, 1)
            pool.wait_ge(ones_ready, 1)
            pool.wait_ge(biases_landed, 2 * 16)
            for c in range(2 * KC):
                last = nc.gpsimd.tensor_scalar(b_wide[:, c, :], ones[:], b_cols[:, c:c + 1], None, ALU.mult)
            last.then_inc(b_wide_ready, 1)
            pool.wait_ge(bias_ready, 1)

            with pool.Fori(0, T) as t:
                pool.wait_ge(zs_copied, t + 1)
                nc.gpsimd.tensor_tensor(row(s_sb, t), row(s_sb, t), bias[:], ALU.add).then_inc(bias_added, 1)

        @block.scalar
        def _(act):
            def normalise(t, k):
                pair, q = k // GROUP, k % GROUP
                nc.scalar.activation(h[:, k % 2, :], row(x_sb, t), ACT.Relu, bias=shift[:, pair, q:q + 1],
                                     scale=rstd[:, pair, q:q + 1]).then_inc(h_ready, 1)

            def take_ht(t, b):
                act.wait_ge(ht_in_psum, t + 1)
                nc.scalar.copy(h_t[:, b].rearrange("p c n -> p (c n)"), ps_ht[b][:, 0:D]).then_inc(ht_ready, 1)

            def copy_zs(t, b):
                act.wait_ge(zs_in_psum, t + 1)
                nc.scalar.copy(row(z, t)[:, 0:D], ps_zs[b][:, 0:D])
                nc.scalar.copy(row(s_sb, t), ps_zs[b][:, D:2 * D]).then_inc(zs_copied, 1)

            def deviation(group):
                act.wait_ge(var_ready, group + 1)
                nc.scalar.activation(std[:], var_eps[:], ACT.Sqrt).then_inc(std_ready, 1)

            def step(t, k):
                before = t if isinstance(t, int) else T
                if k % GROUP == 0:
                    act.wait_ge(shift_ready, t + GROUP)
                if before >= 2:
                    act.wait_ge(ht_in_psum, t - 1)
                normalise(t, k)
                if before >= 3:
                    act.wait_ge(zs_in_psum, t - 2)
                if before >= 1:
                    take_ht(t - 1, (k - 1) % 2)
                if before >= 2:
                    copy_zs(t - 2, (k - 2) % Z_BANKS)

            deviation(0)
            step(0, 0)
            step(1, 1)
            act.wait_ge(ws_folded, 1)
            for c in range(KC):
                last = nc.scalar.copy(w_fold[:, c, D:2 * D], ps_ws[c][:, 0:D])
            last.then_inc(ws_ready, 1)
            step(2, 2)
            deviation(1)
            for t in range(3, BODY - 1):
                step(t, t)
            with act.Fori(1, T // BODY) as turn:
                deviation(turn * 2)
                step(turn * BODY - 1, BODY - 1)
                for k in range(0, 3):
                    step(turn * BODY + k, k)
                deviation(turn * 2 + 1)
                for k in range(3, BODY - 1):
                    step(turn * BODY + k, k)
            step(T - 1, BODY - 1)
            act.wait_ge(zs_in_psum, T - 2)
            take_ht(T - 1, 1)
            copy_zs(T - 2, (T - 2) % Z_BANKS)
            copy_zs(T - 1, (T - 1) % Z_BANKS)

            def take_low_sum(t, b):
                act.wait_ge(tile_summed, t + 1)
                nc.scalar.copy(low_sum, acc[b][:, D:2 * D]).then_inc(low_sum_ready, 1)

            def to_mask(turn, k):
                for slot in (2 * k, 2 * k + 1):
                    act.wait_ge(raw_landed[slot], turn * 16 + 16)
                    nc.scalar.activation(mask_halves[:, slot, :], raw[:, slot, :], ACT.Sigmoid, bias=steep_bias[:],
                                         scale=2 * STEEP).then_inc(converted, 1)

            act.wait_ge(steep_bias_ready, 1)
            nc.scalar.activation(std[:, 0:1], steep_bias[:], ACT.Sigmoid)
            with act.Fori(0, T // MASKS - 1) as turn:
                for k in range(MASKS):
                    take_low_sum(turn * MASKS + k, k % 2)
                    to_mask(turn, k)
                act.wait_ge(out_ready, (turn + 1) * MASKS)
                act.dma_start(out_dram[:, bass.ds(turn * MASKS, MASKS), :],
                              x_sb[:, bass.ds(turn * MASKS, MASKS), :]).then_inc(stored, 16)
            for t in range(T - MASKS, T):
                take_low_sum(t, t % 2)
                act.wait_ge(out_ready, t + 1)
                act.dma_start(out_dram[:, t, :], x_sb[:, t, :]).then_inc(stored, 16)
            act.wait_ge(stored, 16 * (T // MASKS - 1 + MASKS))

        @block.vector
        def _(dve):
            def take_moments(group):
                for q in range(GROUP):
                    last = nc.vector.bn_stats(moments[:, q, :], row(x_sb, group * GROUP + q))
                last.then_inc(moments_ready, 1)

            def variance(group):
                dve.wait_ge(moments_ready, group + 1)
                nc.vector.tensor_tensor(mean_sum[:], moments[:, :, 1], moments[:, :, 4], ALU.add)
                nc.vector.tensor_tensor(mean_gap[:], moments[:, :, 1], moments[:, :, 4], ALU.subtract)
                nc.vector.tensor_tensor(square_sum[:], moments[:, :, 2], moments[:, :, 5],
                                        ALU.add).then_inc(sums_ready, 1)
                dve.wait_ge(sums_ready, group + 1)
                nc.vector.tensor_scalar(within[:], square_sum[:], 1.0 / D, EPS, ALU.mult, ALU.add)
                nc.vector.scalar_tensor_tensor(out=between[:], in0=mean_gap[:], scalar=0.25, in1=mean_gap[:],
                                               op0=ALU.mult, op1=ALU.mult).then_inc(parts_ready, 1)
                dve.wait_ge(parts_ready, group + 1)
                nc.vector.tensor_tensor(var_eps[:], within[:], between[:], ALU.add).then_inc(var_ready, 1)

            def normaliser(group, pair, peeled):
                dve.wait_ge(std_ready, group + 1)
                nc.vector.reciprocal(r0[:], std[:]).then_inc(r0_ready, 1)
                dve.wait_ge(r0_ready, group + 1)
                nc.vector.tensor_tensor(newton_a[:], var_eps[:], r0[:], ALU.mult).then_inc(newton_a_ready, 1)
                dve.wait_ge(newton_a_ready, group + 1)
                nc.vector.scalar_tensor_tensor(out=newton_b[:], in0=newton_a[:], scalar=-0.5, in1=r0[:],
                                               op0=ALU.mult, op1=ALU.mult).then_inc(newton_b_ready, 1)
                dve.wait_ge(newton_b_ready, group + 1)
                if not peeled:
                    dve.wait_ge(h_ready, (group - 1) * GROUP)
                nc.vector.scalar_tensor_tensor(out=rstd[:, pair, :], in0=newton_b[:], scalar=1.5, in1=r0[:],
                                               op0=ALU.add, op1=ALU.mult).then_inc(rstd_ready, 1)
                dve.wait_ge(rstd_ready, group + 1)
                nc.vector.scalar_tensor_tensor(out=shift[:, pair, :], in0=mean_sum[:], scalar=-0.5,
                                               in1=rstd[:, pair, :], op0=ALU.mult,
                                               op1=ALU.mult).then_inc(shift_ready, GROUP)

            def low_part(t, b):
                dve.wait_ge(zs_copied, t + 1)
                nc.vector.tensor_tensor(row(z, t)[:, D:2 * D], ps_zs[b][:, 0:D], row(z, t)[:, 0:D],
                                        ALU.subtract).then_inc(zs_taken, 1)

            def to_mask(half):
                nc.vector.tensor_scalar(row(mask_halves, half), row(raw, half), 0, None,
                                        ALU.is_gt).then_inc(converted, 1)

            nc.vector.memset(ones_column[:], 1.0)
            nc.vector.memset(ones[:], 1.0).then_inc(ones_ready, 1)
            dve.wait_ge(x_landed[0], 16)
            take_moments(0)
            variance(0)
            normaliser(0, 0, True)
            dve.wait_ge(wn_folded, 1)
            for c in range(KC):
                last = nc.vector.tensor_scalar(abs_wn[:, c, :].bitcast(I32), ps_wn[c][:, 0:D].bitcast(I32),
                                               MAGNITUDE, None, ALU.bitwise_and)
            last.then_inc(abs_ready, 1)
            dve.wait_ge(colsum_ready, 1)
            nc.vector.tensor_scalar(share, ps_colsum[:, 0:D], TINY, 1.0 / LIMIT,
                                    ALU.max, ALU.mult).then_inc(share_ready, 1)
            dve.wait_ge(share_ready, 1)
            nc.vector.tensor_scalar(unscale[:].bitcast(I32), share.bitcast(I32), EXPONENT, None,
                                    ALU.bitwise_and).then_inc(unscale_ready, 1)
            dve.wait_ge(unscale_ready, 1)
            nc.vector.tensor_scalar(rescale.bitcast(I32), unscale[:].bitcast(I32), -1.0, float(INVERSE),
                                    ALU.mult, ALU.add).then_inc(rescale_ready, 1)
            dve.wait_ge(rescale_ready, 1)
            for c in range(KC):
                last = nc.vector.tensor_tensor(w_fold[:, c, 0:D], ps_wn[c][:, 0:D], rescale, ALU.mult)
            last.then_inc(wn_ready, 1)
            dve.wait_ge(bias_summed, 1)
            nc.vector.tensor_tensor(bias[:], ps_bias[:, 0:D], b_comb_bc, ALU.add).then_inc(bias_ready, 1)
            dve.wait_ge(x_landed[1], 16)
            take_moments(1)
            variance(1)
            normaliser(1, 1, True)
            for t in range(0, GROUP - 1):
                low_part(t, t % Z_BANKS)
            with dve.Fori(1, T // BODY) as turn:
                dve.wait_ge(x_landed[0], turn * 16 + 16)
                take_moments(turn * 2)
                variance(turn * 2)
                normaliser(turn * 2, 0, False)
                dve.wait_ge(early_landed[0], turn * 16)
                to_mask(turn * 2 - 2)
                for t in range(-GROUP - 1, -1):
                    low_part(turn * BODY + t, t % Z_BANKS)
                dve.wait_ge(x_landed[1], turn * 16 + 16)
                take_moments(turn * 2 + 1)
                variance(turn * 2 + 1)
                normaliser(turn * 2 + 1, 1, False)
                dve.wait_ge(early_landed[1], turn * 16)
                to_mask(turn * 2 - 1)
                for t in range(-1, GROUP - 1):
                    low_part(turn * BODY + t, t % Z_BANKS)
            for t in range(T - GROUP - 1, T):
                low_part(t, t % Z_BANKS)
            for half in (RAWS - 2, RAWS - 1):
                dve.wait_ge(early_landed[half % 2], 16 * RAWS // 2)
                to_mask(half)

            def count(t, k):
                dve.wait_ge(converted, t * 2 + 2)
                for level in range(LEVELS):
                    width = HALF >> level
                    if level == 0:
                        left, right = mask[:, k, 0:HALF], mask[:, k, HALF:2 * HALF]
                    else:
                        dve.wait_ge(counts_step[level - 1], t + 1)
                        left, right = block_sums[:, 0:width], block_sums[:, width:2 * width]
                    target = block_sums[:, 0:width] if level < LEVELS - 1 else counts[:, k % 2, :]
                    nc.vector.tensor_tensor(target, left, right, ALU.add).then_inc(counts_step[level], 1)

            def finish(t, b):
                dve.wait_ge(deg_summed, t + 1)
                nc.vector.tensor_scalar(deg[:], ps_deg[b][:, 0:1], 1.0, None, ALU.max).then_inc(deg_ready, 1)
                dve.wait_ge(deg_ready, t + 1)
                nc.vector.reciprocal(rdeg[:], deg[:]).then_inc(rdeg_ready, 1)
                dve.wait_ge(low_sum_ready, t + 1)
                nc.vector.tensor_tensor(whole_sum, acc[b][:, 0:D], low_sum, ALU.add).then_inc(whole_sum_ready, 1)
                dve.wait_ge(rdeg_ready, t + 1)
                dve.wait_ge(whole_sum_ready, t + 1)
                nc.vector.scalar_tensor_tensor(out=scaled, in0=whole_sum, scalar=rdeg[:], in1=unscale[:],
                                               op0=ALU.mult, op1=ALU.mult).then_inc(scaled_ready, 1)
                dve.wait_ge(scaled_ready, t + 1)
                nc.vector.tensor_tensor(pre, scaled, row(s_sb, t), ALU.add).then_inc(pre_ready, 1)
                dve.wait_ge(pre_ready, t + 1)
                nc.vector.scalar_tensor_tensor(out=row(x_sb, t), in0=pre, scalar=0.0, in1=row(x_sb, t),
                                               op0=ALU.max, op1=ALU.add).then_inc(out_ready, 1)

            dve.wait_ge(bias_added, T)
            with dve.Fori(0, T // MASKS) as turn:
                for k in range(MASKS):
                    count(turn * MASKS + k, k)
                    finish(turn * MASKS + k, k % 2)

        @block.tensor
        def _(pe):
            pe.wait_ge(ones_ready, 1)
            for _ in range(WARM_UP):
                nc.tensor.matmul(ps_bias[:, 0:P], ones[:], ones[:], start=True, stop=True)

            def fold(w_t, offset, target, c):
                for m in range(KC):
                    last = nc.tensor.matmul(target[c][:, 0:D], w_t[:, m, c * P:(c + 1) * P], wc[:, offset + m, :],
                                            start=(m == 0), stop=(m == KC - 1))
                return last

            pe.wait_ge(wn_landed, 2 * 16)
            for c in range(KC):
                last = fold(wn_t, KC, ps_wn, c)
            last.then_inc(wn_folded, 1)

            def transpose_h(t, b):
                pe.wait_ge(h_ready, t + 1)
                for c in range(KC):
                    last = nc.tensor.transpose(ps_ht[b][:, c * P:(c + 1) * P], h[:, b, c * P:(c + 1) * P], ident[:])
                last.then_inc(ht_in_psum, 1)

            def products(t, b, bank):
                pe.wait_ge(ht_ready, t + 1)
                for c in range(KC):
                    last = nc.tensor.matmul(ps_zs[bank][:, :], h_t[:, b, c, :], w_fold[:, c, :],
                                            start=(c == 0), stop=(c == KC - 1))
                last.then_inc(zs_in_psum, 1)

            pe.wait_ge(ident_ready, 1)
            transpose_h(0, 0)
            transpose_h(1, 1)
            pe.wait_ge(abs_ready, 1)
            for c in range(KC):
                last = nc.tensor.matmul(ps_colsum[:, 0:D], ones[:], abs_wn[:, c, :],
                                        start=(c == 0), stop=(c == KC - 1))
            last.then_inc(colsum_ready, 1)
            pe.wait_ge(ws_landed, 2 * 16)
            for c in range(KC):
                last = fold(ws_t, 0, ps_ws, c)
            last.then_inc(ws_folded, 1)
            pe.wait_ge(b_wide_ready, 1)
            for c in range(2 * KC):
                last = nc.tensor.matmul(ps_bias[:, 0:D], b_wide[:, c, :], wc[:, c, :],
                                        start=(c == 0), stop=(c == 2 * KC - 1))
            last.then_inc(bias_summed, 1)
            pe.wait_ge(wn_ready, 1)
            pe.wait_ge(ws_ready, 1)
            products(0, 0, 0)

            def step(t, k):
                pe.wait_ge(ht_ready, t - 1)
                transpose_h(t, k % 2)
                if not isinstance(t, int) or t > Z_BANKS:
                    pe.wait_ge(zs_taken, t - Z_BANKS)
                products(t - 1, (k - 1) % 2, (k - 1) % Z_BANKS)

            for t in range(2, BODY):
                step(t, t)
            with pe.Fori(1, T // BODY) as turn:
                for k in range(BODY):
                    step(turn * BODY + k, k)
            pe.wait_ge(zs_taken, T - Z_BANKS)
            products(T - 1, 1, (T - 1) % Z_BANKS)

            def sum_tile(t, k):
                peeled = isinstance(t, int)
                b = k % 2
                if not peeled or k >= 2:
                    pe.wait_ge(scaled_ready, t - 1)
                for j in range(T):
                    if j % (T // 2) == 0:
                        pe.wait_ge(converted, t * 2 + (1 + j // (T // 2)))
                    if peeled and k == 0 and j >= T - GROUP - 1:
                        pe.wait_ge(zs_taken, j + 1)
                    last = nc.tensor.matmul(acc[b][:, :], mask[:, k, j * P:(j + 1) * P], z[:, j, :],
                                            start=(j == 0), stop=(j == T - 1))
                    if j == T - 2:
                        pe.wait_ge(counts_step[LEVELS - 1], t + 1)
                        nc.tensor.matmul(ps_deg[b][:, 0:1], counts[:, b, :], ones_column[:],
                                         start=True, stop=True).then_inc(deg_summed, 1)
                last.then_inc(tile_summed, 1)

            for k in range(MASKS):
                sum_tile(k, k)
            with pe.Fori(1, T // MASKS) as turn:
                for k in range(MASKS):
                    sum_tile(turn * MASKS + k, k)


def kernel(x, adj, L0_gnn_W_self, L0_gnn_b_self, L0_gnn_W_nb, L0_gnn_b_nb, L0_gnn_W_comb, L0_gnn_b_comb):
    import numpy as np
    import concourse.bacc as bacc
    from concourse.bass_utils import run_bass_kernel_spmd

    x, adj = np.asarray(x), np.asarray(adj)
    N, D = x.shape
    T, KC = N // P, D // P
    adj_t = adj.reshape(P, T, P, 2, T // 2).transpose(1, 3, 2, 4, 0).reshape(2 * T, P, N // 2)
    columns = [np.asarray(b).reshape(KC, P).T for b in (L0_gnn_b_self, L0_gnn_b_nb)]
    arrays = {
        "x": x,
        "adj_t": adj_t,
        "w_self_t": np.asarray(L0_gnn_W_self).T,
        "w_nb_t": np.asarray(L0_gnn_W_nb).T,
        "w_comb": np.asarray(L0_gnn_W_comb),
        "b_hidden": np.concatenate(columns, axis=1),
        "b_comb": np.asarray(L0_gnn_b_comb).reshape(1, D),
    }
    arrays = {name: np.ascontiguousarray(a) for name, a in arrays.items()}

    nc = bacc.Bacc("TRN2", target_bir_lowering=False, num_devices=1)
    ins = [nc.dram_tensor(name, a.shape, mybir.dt.from_np(a.dtype), kind="ExternalInput").ap()
           for name, a in arrays.items()]
    out = nc.dram_tensor("out", (N, D), F32, kind="ExternalOutput").ap()
    gnn_kernel(nc, *ins, out)
    return run_bass_kernel_spmd(nc, [arrays], core_ids=[0]).results[0]["out"]
```
